# Optimizing a Trainium2 kernel written in Bass

```python
import numpy as np
import jax
import jax.numpy as jnp

def _softmax(x, axis=-1):
    return jax.nn.softmax(x, axis=axis)

def _gelu(x):
    return jax.nn.gelu(x, approximate=True)

def _silu(x):
    return jax.nn.silu(x)

def _sigmoid(x):
    return jax.nn.sigmoid(x)

def _layernorm(x, axis=-1, eps=1e-05):
    m = jnp.mean(x, axis=axis, keepdims=True)
    v = jnp.var(x, axis=axis, keepdims=True)
    return (x - m) / jnp.sqrt(v + eps)

def _scatter_add(tgt, idx, src, axis=0):
    return tgt.at[idx].add(src)

def _segment_sum(src, seg, n):
    return jax.ops.segment_sum(src, seg, n)
kernel_name = 'mk_adj_resnorm_d1_adj_r2_2dc59d'

def setup_inputs(seed: int=0):
    np.random.seed(seed)
    _w = jnp.asarray

    def _rec_inputs():
        import jax
        import jax.numpy as jnp
        _gk = jax.random.key(seed)
        x = 0.0002141 + 1 * jax.random.normal(jax.random.fold_in(_gk, 1), (128, 64, 384), jnp.float32)
        _a = jax.random.bernoulli(jax.random.fold_in(_gk, 2), 0.125, (128, 64, 64))
        _a = jnp.logical_or(_a, jnp.eye(64, dtype=bool))
        adj = _a.astype(jnp.int32)
        return (x, adj)
    x, adj = _rec_inputs()

    def _L0_gnn_setup():
        import jax, jax.numpy as jnp
        import numpy as np
        B, S, HID, DEP, DS, NTYPES = (8, 128, 384, 64, 384, 45)
        NEG = -1000000000.0
        key = jax.random.key(seed)
        ks = jax.random.split(key, 10)
        sc = lambda fan_in: 1.0 / np.sqrt(fan_in)
        return {'h': jax.random.normal(ks[0], (B, S, HID), dtype=jnp.float32), 'dep_type_matrix': jax.random.randint(ks[1], (B, S, S), 0, NTYPES), 'dep_emb_table': jax.random.normal(ks[2], (NTYPES, DEP), dtype=jnp.float32), 'W1_w': jax.random.normal(ks[3], (HID + DEP, DS), dtype=jnp.float32) * sc(HID + DEP), 'W1_b': jnp.zeros((DS,), dtype=jnp.float32), 'W2_w': jax.random.normal(ks[4], (HID + DEP, DS), dtype=jnp.float32) * sc(HID + DEP), 'W2_b': jnp.zeros((DS,), dtype=jnp.float32), 'gcn_w': jax.random.normal(ks[5], (HID, HID), dtype=jnp.float32) * sc(HID), 'gcn_b': jnp.zeros((HID,), dtype=jnp.float32), 'Wo_w': jax.random.normal(ks[6], (DS, HID), dtype=jnp.float32) * sc(DS), 'Wo_b': jnp.zeros((HID,), dtype=jnp.float32)}
    _L0_gnn_all = _L0_gnn_setup()
    _L0_gnn_in = {k: v for k, v in _L0_gnn_all.items() if k in ('dep_emb_table', 'W1_w', 'W1_b', 'W2_w', 'W2_b', 'gcn_w', 'gcn_b', 'Wo_w', 'Wo_b')}
    del _L0_gnn_all
    return {'x': x, 'adj': adj, 'L0_gnn_dep_emb_table': _L0_gnn_in['dep_emb_table'], 'L0_gnn_W1_w': _L0_gnn_in['W1_w'], 'L0_gnn_W1_b': _L0_gnn_in['W1_b'], 'L0_gnn_W2_w': _L0_gnn_in['W2_w'], 'L0_gnn_W2_b': _L0_gnn_in['W2_b'], 'L0_gnn_gcn_w': _L0_gnn_in['gcn_w'], 'L0_gnn_gcn_b': _L0_gnn_in['gcn_b'], 'L0_gnn_Wo_w': _L0_gnn_in['Wo_w'], 'L0_gnn_Wo_b': _L0_gnn_in['Wo_b']}

def reference(x, adj, L0_gnn_dep_emb_table, L0_gnn_W1_w, L0_gnn_W1_b, L0_gnn_W2_w, L0_gnn_W2_b, L0_gnn_gcn_w, L0_gnn_gcn_b, L0_gnn_Wo_w, L0_gnn_Wo_b):
    import jax
    import jax.numpy as jnp

    def _L0_gnn_ref(h, dep_type_matrix, dep_emb_table, W1_w, W1_b, W2_w, W2_b, gcn_w, gcn_b, Wo_w, Wo_b):
        import jax, jax.numpy as jnp
        import numpy as np
        B, S, HID, DEP, DS, NTYPES = (8, 128, 384, 64, 384, 45)
        NEG = -1000000000.0
        adj = dep_type_matrix != 0
        dep_emb = dep_emb_table[dep_type_matrix]
        hi_t = jnp.einsum('bid,de->bie', h, W1_w[:HID])[:, :, None, :] + jnp.einsum('bijd,de->bije', dep_emb, W1_w[HID:]) + W1_b
        hj_t = jnp.einsum('bjd,de->bje', h, W2_w[:HID])[:, None, :, :] + jnp.einsum('bijd,de->bije', dep_emb, W2_w[HID:]) + W2_b
        relevance = jnp.sum(hi_t * hj_t, axis=-1)
        masked = jnp.where(adj, relevance, NEG)
        A = jax.nn.softmax(masked, axis=2)
        h_syn = h
        for _ in range(1):
            aggregated = jnp.einsum('bij,bjd->bid', A, h_syn)
            h_syn = jax.nn.relu(aggregated @ gcn_w + gcn_b)
        return h_syn @ Wo_w + Wo_b
    x = _layernorm(x + _L0_gnn_ref(x, adj, L0_gnn_dep_emb_table, L0_gnn_W1_w, L0_gnn_W1_b, L0_gnn_W2_w, L0_gnn_W2_b, L0_gnn_gcn_w, L0_gnn_gcn_b, L0_gnn_Wo_w, L0_gnn_Wo_b), axis=-1)
    return x

_drawn_inputs = setup_inputs


def setup_inputs(seed=0):
    import zlib

    import numpy as np

    out = dict(_drawn_inputs(seed))
    spreads = {'L0_gnn_W1_b': (0.0, 0.1),
     'L0_gnn_W2_b': (0.0, 0.1),
     'L0_gnn_gcn_b': (0.0, 0.1),
     'L0_gnn_Wo_b': (0.0, 0.1)}
    factors = {}
    for name, (base, spread) in spreads.items():
        noise = np.random.default_rng([zlib.crc32(name.encode()), seed]).standard_normal(out[name].shape)
        drawn = base * np.exp(spread * noise) if base else spread * noise
        out[name] = jnp.asarray(drawn.astype(out[name].dtype))
    for name, factor in factors.items():
        out[name] = (out[name] * factor).astype(out[name].dtype)
    return out
```

```python
from contextlib import ExitStack

import concourse.bass as bass
from concourse import mybir

ALU = mybir.AluOpType
ACT = mybir.ActivationFunctionType
AX = mybir.AxisListType
F32 = mybir.dt.float32
F32R = mybir.dt.float32r
I32 = mybir.dt.int32

P = 128
NEG = -1000000000.0
LN_EPS = 1e-05


def adj_resnorm_kernel(
    nc: bass.Bass,
    xT: bass.AP,
    xn: bass.AP,
    adj: bass.AP,
    embT: bass.AP,
    w1T: bass.AP,
    w2T: bass.AP,
    wdep: bass.AP,
    gcn_w: bass.AP,
    wo_w: bass.AP,
    bias_cols: bass.AP,
    wo_b: bass.AP,
    out: bass.AP,
):
    GROUPS, _, KC, TOK = xT.shape
    HID = KC * P
    TILES = TOK // P
    NODES = adj.shape[3]
    TYPES = embT.shape[1]
    DEP = embT.shape[0]
    YW = HID + 2

    ctx = ExitStack()
    with ctx:
        def sb(name, shape, dt=F32):
            return ctx.enter_context(nc.sbuf_tensor(name, shape, dt))

        def ps(name, shape):
            return ctx.enter_context(nc.psum_tensor(name, shape, F32))

        def sem(name):
            return ctx.enter_context(nc.semaphore(name))

        w1T_sb = sb("w1T_sb", [P, KC, HID])
        w2T_sb = sb("w2T_sb", [P, KC, HID])
        wdep_sb = sb("wdep_sb", [DEP, 2, HID])
        embT_sb = sb("embT_sb", [DEP, TYPES])
        gcn_sb = sb("gcn_sb", [P, KC, YW])
        wo_sb = sb("wo_sb", [P, KC, HID])
        bias_sb = sb("bias_sb", [P, 3, KC])
        wo_b_sb = sb("wo_b_sb", [P, HID])
        ones = sb("ones", [P, P])
        ident = sb("ident", [P, P])
        minus_half = sb("minus_half", [P, TILES])
        c1 = sb("c1", [P, KC, TYPES])
        c2 = sb("c2", [P, KC, TYPES])
        c12 = sb("c12", [P, KC, TYPES])
        w2c1 = sb("w2c1", [P, KC, TYPES])
        w1c2 = sb("w1c2", [P, KC, TYPES])
        c1c2 = sb("c1c2", [P, TYPES])
        m_sb = sb("m_sb", [P, KC, HID])
        m_hi = sb("m_hi", [P, KC, HID], F32R)
        m_lo = sb("m_lo", [P, KC, HID], F32R)
        gcn_hi = sb("gcn_hi", [P, KC, YW], F32R)
        gcn_lo = sb("gcn_lo", [P, KC, YW], F32R)
        wo_hi = sb("wo_hi", [P, KC, HID], F32R)
        wo_lo = sb("wo_lo", [P, KC, HID], F32R)
        adj_sb = sb("adj_sb", [P, GROUPS, TILES, NODES], I32)

        xT_sb = [sb(f"xT_sb{p}", [P, KC, TOK]) for p in range(2)]
        xT_hi = [sb(f"xT_hi{p}", [P, KC, TOK], F32R) for p in range(2)]
        xT_lo = [sb(f"xT_lo{p}", [P, KC, TOK], F32R) for p in range(2)]
        xb = [sb(f"xb{p}", [P, TILES, HID]) for p in range(2)]
        z_sb = sb("z_sb", [P, KC, TOK])
        y_sb = sb("y_sb", [P, TILES, YW])
        row_term = sb("row_term", [P, TILES])
        neg_mask = sb("neg_mask", [P, TILES, NODES])
        rel = sb("rel", [P, TILES, NODES])
        rel_kept = sb("rel_kept", [P, TILES, NODES])
        masked = sb("masked", [P, TILES, NODES])
        neg_max = sb("neg_max", [P, TILES])
        expd = sb("expd", [P, TILES, NODES])
        exp_sum = sb("exp_sum", [P, TILES])
        exp_inv = sb("exp_inv", [P, TILES])
        attn = sb("attn", [P, TILES, P])
        attnT = sb("attnT", [P, TOK])
        h_sb = sb("h_sb", [P, KC, TOK])
        h_hi = sb("h_hi", [P, KC, TOK], F32R)
        h_lo = sb("h_lo", [P, KC, TOK], F32R)
        res = sb("res", [P, TILES, HID])
        stats = sb("stats", [P, TILES, 6])
        mean_var = sb("mean_var", [P, TILES, 2])
        var_eps = sb("var_eps", [P, TILES])
        rstd = sb("rstd", [P, TILES])
        normed = [sb(f"normed{p}", [P, TILES, HID]) for p in range(2)]

        type_max = sb("type_max", [P, TILES, NODES], I32)
        type_col = sb("type_col", [P, 1])
        type_all = sb("type_all", [P, 1])
        type_flag = sb("type_flag", [P, 1], I32)
        type_ids = sb("type_ids", [P, TYPES])
        type_iota = sb("type_iota", [P, TYPES], I32)

        t_xT = xT_sb[0][:, :, 0:P]
        t_x = xb[0][:, 0, :]
        t_xb = xb[0][:, 1, :]
        t_out = normed[0][:, 0, :]
        t_sq = normed[0][:, 1, :]
        t_z = xT_sb[1][:, :, 0:P]
        t_zt = xT_sb[1][:, :, P:2 * P]
        t_h = xT_sb[1][:, :, 2 * P:3 * P]
        t_y = res[:, 1, :]
        t_res = res[:, 0, :]
        t_centred = res[:, 2, :]
        t_attnT = res[:, 3, 0:P]
        t_adj = rel[:, 0, :]
        t_rel = rel_kept[:, 0, :]
        t_picked = rel_kept[:, 1, :]
        t_sum = masked[:, 0, :]
        t_neg = masked[:, 1, :]
        t_masked = masked[:, 2, :]
        t_exp = expd[:, 0, :]
        t_row = sb("t_row", [P, TYPES])
        t_small = sb("t_small", [P, 8])
        t_neg_max, t_exp_sum, t_exp_inv, t_total, t_mean, t_sqsum, t_var, t_rstd = (
            t_small[:, k:k + 1] for k in range(8))

        att_ps = ps("att_ps", [P, TILES, P])
        col_ps = [ps(f"col_ps{c}", [P, TOK]) for c in range(KC)]
        row_ps = ps("row_ps", [P, TILES, 512])

        w1_in, w2_in, small_in, gcn_in, wo_in, adj_in, wo_b_in = (
            sem(n) for n in ("w1_in", "w2_in", "small_in", "gcn_in", "wo_in", "adj_in", "wo_b_in"))
        xT_in = [sem(f"xT_in{p}") for p in range(2)]
        xn_in = [sem(f"xn_in{p}") for p in range(2)]
        stored = [sem(f"stored{p}") for p in range(2)]
        consts_ready, c_ps_done, c_ready, table_ps_done, table_ready, m_ps_done, m_ready, w_split = (
            sem(n) for n in ("consts_ready", "c_ps_done", "c_ready", "table_ps_done", "table_ready",
                             "m_ps_done", "m_ready", "w_split"))
        gcn_split, wo_split, attn_zeroed = sem("gcn_split"), sem("wo_split"), sem("attn_zeroed")
        x_hi_ready = sem("x_hi_ready")
        x_lo_ready = sem("x_lo_ready")
        xb_ready = sem("xb_ready")
        z_done = sem("z_done")
        z_ready = sem("z_ready")
        y_done = sem("y_done")
        y_ready = sem("y_ready")
        row_ready = sem("row_ready")
        rel_done = sem("rel_done")
        neg_mask_ready = sem("neg_mask_ready")
        soft_step = sem("soft_step")
        max_ready = sem("max_ready")
        exp_done = sem("exp_done")
        inv_ready = sem("inv_ready")
        attn_ready = sem("attn_ready")
        attnT_done = sem("attnT_done")
        attnT_ready = sem("attnT_ready")
        h_done = sem("h_done")
        relu_done = sem("relu_done")
        h_hi_ready = sem("h_hi_ready")
        h_lo_ready = sem("h_lo_ready")
        out_done = sem("out_done")
        res_ready = sem("res_ready")
        stats_ready = sem("stats_ready")
        aggr_ready = sem("aggr_ready")
        var_ready = sem("var_ready")
        rstd_ready = sem("rstd_ready")
        norm_done = sem("norm_done")

        type_max_ready = sem("type_max_ready")
        type_all_ready = sem("type_all_ready")
        type_flag_ready = sem("type_flag_ready")
        type_zeroed = sem("type_zeroed")
        t_in = sem("t_in")
        t_front_done = sem("t_front_done")
        t_rel_done = sem("t_rel_done")
        t_exp_done = sem("t_exp_done")
        t_attnT_done = sem("t_attnT_done")
        t_h_done = sem("t_h_done")
        t_relu_done = sem("t_relu_done")
        t_out_done = sem("t_out_done")
        t_rstd_ready = sem("t_rstd_ready")
        t_vec = sem("t_vec")
        t_stored = sem("t_stored")

        T_FRONT, T_TYPE, T_REST = KC + 5, KC + 4, 15
        EDGE_TYPES = TYPES - 1
        T_ALL = T_FRONT + EDGE_TYPES * T_TYPE + T_REST

        def typed_pass(eng, tile, stores=False):
            eng.wait_ge(type_flag_ready, 1)
            greatest = eng.value_load(type_flag[0:1, 0:1], min_val=0, max_val=TYPES - 1)
            with eng.If(greatest > 1):
                with eng.Fori(0, GROUPS) as g:
                    with eng.Fori(0, TILES) as q:
                        tile(g, q, TILES * g + q)
                if stores:
                    eng.wait_ge(t_stored, 16 * GROUPS * TILES)

        FIRST_LOOPED, LAST_LOOPED = 3, GROUPS - 4

        def run_steps(eng, step):
            for g in range(FIRST_LOOPED):
                step(g, g % 2)
            with eng.Fori(0, (LAST_LOOPED - FIRST_LOOPED + 1) // 2) as i:
                for g in range(FIRST_LOOPED, FIRST_LOOPED + 2):
                    step(2 * i + g, g % 2, True)
            for g in range(LAST_LOOPED + 1, GROUPS + 1):
                step(g, g % 2)

        block = ctx.enter_context(nc.Block())

        @block.sync
        def _(sp):
            sp.dma_start(w1T_sb[:], w1T).then_inc(w1_in, 16)
            sp.dma_start(xT_sb[0][:], xT[0]).then_inc(xT_in[0], 16)
            sp.dma_start(wo_sb[:], wo_w).then_inc(wo_in, 16)
            sp.dma_start(xT_sb[1][:], xT[1]).then_inc(xT_in[1], 16)
            sp.dma_start(adj_sb[:].rearrange("p g t n -> p g (t n)"),
                         adj.rearrange("g p t n -> p g (t n)")).then_inc(adj_in, 16)
            sp.dma_start(xb[0][:], xn[0]).then_inc(xn_in[0], 16)
            sp.dma_start(xb[1][:], xn[1]).then_inc(xn_in[1], 16)

            def step(g, p, looped=False):
                if looped or g + 2 < GROUPS:
                    sp.wait_ge(rel_done, g + 1)
                    sp.dma_start(xT_sb[p][:], xT[g + 2]).then_inc(xT_in[p], 16)
                if looped or 1 <= g <= GROUPS - 2:
                    sp.wait_ge(res_ready, TILES * g)
                    sp.dma_start(xb[1 - p][:], xn[g + 1]).then_inc(xn_in[1 - p], 16)
                if looped or g >= 1:
                    sp.wait_ge(norm_done, TILES * g)
                    sp.dma_start(out[g - 1], normed[1 - p][:]).then_inc(stored[1 - p], 16)
            run_steps(sp, step)
            for p in range(2):
                sp.wait_ge(stored[p], 16 * (GROUPS // 2))

            def typed_tile(g, q, n):
                sp.dma_start(t_xT, xT[g, :, :, bass.ds(q * P, P)]).then_inc(t_in, 16)
                sp.dma_start(t_x, xn[g, :, bass.ds(q, 1), :].rearrange("p o d -> p (o d)")).then_inc(t_in, 16)
                sp.wait_ge(t_vec, T_ALL * (n + 1))
                sp.dma_start(out[g, :, bass.ds(q, 1), :].rearrange("p o d -> p (o d)"), t_out).then_inc(t_stored, 16)

            typed_pass(sp, typed_tile, stores=True)

        @block.gpsimd
        def _(pool):
            nc.gpsimd.memset(ident[:], 0.0).then_inc(consts_ready, 1)
            nc.gpsimd.memset(ones[:], 1.0).then_inc(consts_ready, 1)
            nc.gpsimd.memset(minus_half[:], -0.5).then_inc(consts_ready, 1)
            pool.wait_ge(consts_ready, 1)
            nc.gpsimd.affine_select(out=ident[:], in_=ident[:], compare_op=ALU.not_equal, fill=1.0, base=0,
                                    pattern=[[-1, P]], channel_multiplier=1).then_inc(consts_ready, 1)
            nc.gpsimd.memset(attn[:], 0.0).then_inc(attn_zeroed, 1)
            nc.gpsimd.memset(type_max[:], 0).then_inc(type_zeroed, 1)
            nc.gpsimd.iota(type_iota[:], pattern=[[1, TYPES]], base=0, channel_multiplier=0).then_inc(type_zeroed, 1)
            def x_lo_part(g, p):
                for c in range(KC):
                    pool.wait_ge(x_hi_ready, KC * g + c + 1)
                    nc.gpsimd.tensor_tensor(xT_lo[p][:, c, :], xT_sb[p][:, c, :], xT_hi[p][:, c, :].bitcast(F32),
                                            ALU.subtract).then_inc(x_lo_ready, 1)

            x_lo_part(0, 0)
            x_lo_part(1, 1)

            def step(g, p, looped=False):
                live = looped or g < GROUPS
                if live:
                    if not looped and g == 0:
                        pool.wait_ge(wo_b_in, 16)
                    pool.wait_ge(xn_in[p], 8 * (g - p) + 16)
                    for t in range(TILES):
                        nc.gpsimd.tensor_tensor(xb[p][:, t, :], xb[p][:, t, :], wo_b_sb[:], ALU.add).then_inc(xb_ready, 1)
                if looped or g + 2 < GROUPS:
                    x_lo_part(g + 2, p)
                if looped or g >= 1:
                    if not looped and g == 1:
                        pool.wait_ge(consts_ready, 3)
                    pool.wait_ge(var_ready, g)
                    nc.gpsimd.tensor_tensor(rstd[:], var_eps[:], minus_half[:], ALU.pow).then_inc(rstd_ready, 1)
                if live:
                    for c in range(KC):
                        pool.wait_ge(h_hi_ready, KC * g + c + 1)
                        nc.gpsimd.tensor_tensor(h_lo[:, c, :], h_sb[:, c, :], h_hi[:, c, :].bitcast(F32),
                                                ALU.subtract).then_inc(h_lo_ready, 1)

            run_steps(pool, step)
            pool.wait_ge(type_max_ready, GROUPS + 1)
            nc.gpsimd.partition_all_reduce(type_all[:], type_col[:], P, bass.bass_isa.ReduceOp.max).then_inc(type_all_ready, 1)

            def typed_tile(g, q, n):
                pool.wait_ge(t_vec, T_ALL * (n + 1) - 1)
                nc.gpsimd.tensor_tensor(t_rstd, t_var, minus_half[:, 0:1], ALU.pow).then_inc(t_rstd_ready, 1)

            typed_pass(pool, typed_tile)

        @block.scalar
        def _(act):
            act.dma_start(w2T_sb[:], w2T).then_inc(w2_in, 16)
            act.dma_start(embT_sb[:], embT).then_inc(small_in, 16)
            act.dma_start(wdep_sb[:], wdep).then_inc(small_in, 16)
            act.dma_start(bias_sb[:], bias_cols).then_inc(small_in, 16)
            act.dma_start(gcn_sb[:, :, 0:HID], gcn_w).then_inc(gcn_in, 16)
            act.dma_start(wo_b_sb[:], wo_b.partition_broadcast(P)).then_inc(wo_b_in, 16)
            for c in range(KC):
                act.wait_ge(m_ps_done, c + 1)
                nc.scalar.activation(m_sb[:, c, :], col_ps[c][:, 0:HID], ACT.Identity).then_inc(m_ready, 1)
            act.wait_ge(m_ready, KC)
            nc.scalar.activation(m_hi[:], m_sb[:], ACT.Identity).then_inc(m_ready, 1)

            def z_part(g):
                for c in range(KC):
                    act.wait_ge(z_done, KC * g + c + 1)
                    nc.scalar.activation(z_sb[:, c, :], col_ps[c][:], ACT.Identity,
                                         bias=w2c1[:, c, 1:2]).then_inc(z_ready, 1)

            def y_part(g):
                for t in range(TILES):
                    act.wait_ge(y_done, TILES * g + t + 1)
                    nc.scalar.activation(y_sb[:, t, :], row_ps[:, t, 0:YW], ACT.Identity).then_inc(y_ready, 1)

            def neg_mask_part(g):
                nc.scalar.activation(neg_mask[:], adj_sb[:, g], ACT.Copy, scale=-NEG,
                                     bias=NEG).then_inc(neg_mask_ready, 1)

            act.wait_ge(table_ready, 3)
            z_part(0)
            y_part(0)
            act.wait_ge(adj_in, 16)
            neg_mask_part(0)

            def step(g, p, looped=False):
                if not looped and g == GROUPS:
                    return
                for t in range(TILES):
                    if t == 0:
                        act.wait_ge(max_ready, g + 1)
                    nc.scalar.activation(expd[:, t, :], masked[:, t, :], ACT.Exp, bias=neg_max[:, t:t + 1],
                                         accum_out=exp_sum[:, t:t + 1]).then_inc(exp_done, 1)
                if looped or g + 1 < GROUPS:
                    neg_mask_part(g + 1)
                    act.wait_ge(rel_done, g + 1)
                    z_part(g + 1)
                act.wait_ge(attnT_done, g + 1)
                if looped or g >= 1:
                    act.wait_ge(h_done, KC * g)
                nc.scalar.activation(attnT[:], att_ps[:].rearrange("p t n -> p (t n)"),
                                     ACT.Identity).then_inc(attnT_ready, 1)
                for c in range(KC):
                    if looped or g >= 1:
                        act.wait_ge(h_lo_ready, KC * (g - 1) + c + 1)
                    act.wait_ge(h_done, KC * g + c + 1)
                    nc.scalar.activation(h_sb[:, c, :], col_ps[c][:], ACT.Relu,
                                         bias=bias_sb[:, 2, c:c + 1]).then_inc(relu_done, 1)
                if looped or g + 1 < GROUPS:
                    y_part(g + 1)

            run_steps(act, step)

            def typed_tile(g, q, n):
                at_rest = T_ALL * n + T_FRONT + EDGE_TYPES * T_TYPE
                act.wait_ge(t_vec, at_rest + 3)
                nc.scalar.activation(t_exp, t_masked, ACT.Exp, bias=t_neg_max,
                                     accum_out=t_exp_sum).then_inc(t_exp_done, 1)
                act.wait_ge(t_h_done, n + 1)
                for c in range(KC):
                    nc.scalar.activation(t_h[:, c, :], col_ps[c][:, 0:P], ACT.Relu,
                                         bias=bias_sb[:, 2, c:c + 1]).then_inc(t_relu_done, 1)

            typed_pass(act, typed_tile)

        @block.vector
        def _(dve):
            dve.wait_ge(small_in, 48)
            for k, table in enumerate((c1, c2)):
                for c in range(KC):
                    dve.wait_ge(c_ps_done, KC * (k + 1))
                    nc.vector.tensor_scalar(table[:, c, :], row_ps[:, k, c * TYPES:(c + 1) * TYPES],
                                            bias_sb[:, k, c:c + 1], None, ALU.add).then_inc(c_ready, 1)
            dve.wait_ge(c_ready, 2 * KC)
            nc.vector.tensor_tensor(c12[:], c1[:], c2[:], ALU.mult).then_inc(c_ready, 1)

            def x_hi_part(g, p):
                for c in range(KC):
                    nc.vector.tensor_copy(xT_hi[p][:, c, :], xT_sb[p][:, c, :]).then_inc(x_hi_ready, 1)

            dve.wait_ge(xT_in[0], 16)
            x_hi_part(0, 0)
            dve.wait_ge(table_ps_done, 3)
            nc.vector.tensor_copy(w2c1[:].rearrange("p c n -> p (c n)"), row_ps[:, 2, 0:KC * TYPES]).then_inc(table_ready, 1)
            nc.vector.tensor_copy(w1c2[:].rearrange("p c n -> p (c n)"), row_ps[:, 3, 0:KC * TYPES]).then_inc(table_ready, 1)
            nc.vector.tensor_copy(c1c2[:], row_ps[:, 0, 256:256 + TYPES]).then_inc(table_ready, 1)
            dve.wait_ge(m_ready, KC + 1)
            nc.vector.tensor_tensor(m_lo[:], m_sb[:], m_hi[:].bitcast(F32), ALU.subtract).then_inc(w_split, 1)
            dve.wait_ge(gcn_in, 16)
            dve.wait_ge(table_ready, 2)
            nc.vector.tensor_copy(gcn_sb[:, :, HID:HID + 1], w1c2[:, :, 1:2]).then_inc(gcn_split, 1)
            nc.vector.memset(gcn_sb[:, :, HID + 1:YW], 0.0).then_inc(gcn_split, 1)
            dve.wait_ge(gcn_split, 2)
            nc.vector.tensor_copy(gcn_hi[:], gcn_sb[:]).then_inc(gcn_split, 1)
            dve.wait_ge(gcn_split, 3)
            nc.vector.tensor_tensor(gcn_lo[:], gcn_sb[:], gcn_hi[:].bitcast(F32), ALU.subtract).then_inc(gcn_split, 1)
            dve.wait_ge(xT_in[1], 16)
            x_hi_part(1, 1)

            def row_part(g):
                dve.wait_ge(y_ready, TILES * (g + 1))
                nc.vector.tensor_scalar(row_term[:], y_sb[:, :, HID:HID + 1].rearrange("p t o -> p (t o)"),
                                        c1c2[:, 1:2], None, ALU.add).then_inc(row_ready, 1)

            row_part(0)
            dve.wait_ge(wo_in, 16)
            nc.vector.tensor_copy(wo_hi[:], wo_sb[:]).then_inc(wo_split, 1)
            dve.wait_ge(wo_split, 1)
            nc.vector.tensor_tensor(wo_lo[:], wo_sb[:], wo_hi[:].bitcast(F32), ALU.subtract).then_inc(wo_split, 1)
            dve.wait_ge(attn_zeroed, 1)
            dve.wait_ge(type_zeroed, 1)

            def residual(g, t):
                dve.wait_ge(out_done, TILES * g + t + 1)
                nc.vector.tensor_tensor(res[:, t, :], row_ps[:, t, 0:HID], xb_of(g, t), ALU.add).then_inc(res_ready, 1)
                dve.wait_ge(res_ready, TILES * g + t + 1)
                nc.vector.bn_stats(stats[:, t, :], res[:, t, :]).then_inc(stats_ready, 1)

            parity = [0]

            def xb_of(g, t):
                return xb[parity[0]][:, t, :]

            def step(g, p, looped=False):
                live = looped or g < GROUPS
                before = looped or g >= 1
                after = looped or g + 1 < GROUPS
                parity[0] = 1 - p
                if live:
                    dve.wait_ge(row_ready, g + 1)
                    dve.wait_ge(rel_done, g + 1)
                    nc.vector.tensor_tensor(rel[:], att_ps[:, :, 0:NODES],
                                            row_term[:].rearrange("p (t o) -> p t o", o=1).to_broadcast([P, TILES, NODES]),
                                            ALU.add).then_inc(soft_step, 1)
                    dve.wait_ge(neg_mask_ready, g + 1)
                    dve.wait_ge(soft_step, 3 * g + 1)
                    nc.vector.tensor_tensor(rel_kept[:], rel[:], adj_sb[:, g], ALU.mult).then_inc(soft_step, 1)
                    if before:
                        dve.wait_ge(type_max_ready, g)
                    nc.vector.tensor_tensor(type_max[:], type_max[:], adj_sb[:, g], ALU.max).then_inc(type_max_ready, 1)
                    dve.wait_ge(soft_step, 3 * g + 2)
                    nc.vector.tensor_tensor(masked[:], rel_kept[:], neg_mask[:], ALU.add).then_inc(soft_step, 1)
                    dve.wait_ge(soft_step, 3 * g + 3)
                    nc.vector.tensor_reduce(neg_max[:], masked[:], AX.X, ALU.max, negate=True).then_inc(max_ready, 1)
                if live:
                    dve.wait_ge(exp_done, TILES * (g + 1))
                    nc.vector.reciprocal(exp_inv[:], exp_sum[:]).then_inc(inv_ready, 1)
                    dve.wait_ge(inv_ready, g + 1)
                    if before:
                        dve.wait_ge(attnT_done, g)
                    for b in range(2):
                        r = slice(b * NODES, (b + 1) * NODES)
                        nc.vector.tensor_tensor(attn[r, :, r], expd[r],
                                                exp_inv[r].rearrange("p (t o) -> p t o", o=1).to_broadcast([NODES, TILES, NODES]),
                                                ALU.mult).then_inc(attn_ready, 1)
                if before:
                    dve.wait_ge(xb_ready, TILES * g)
                    if looped or g >= 2:
                        dve.wait_ge(norm_done, TILES * (g - 1))
                    residual(g - 1, 0)
                    residual(g - 1, 1)
                if looped or g + 2 < GROUPS:
                    dve.wait_ge(xT_in[p], 8 * (g - p) + 32)
                    x_hi_part(g + 2, p)
                if before:
                    residual(g - 1, 2)
                    residual(g - 1, 3)
                if live:
                    for c in range(KC):
                        if c == 0 and before:
                            dve.wait_ge(out_done, TILES * g)
                            dve.wait_ge(stats_ready, TILES * g)
                        dve.wait_ge(relu_done, KC * g + c + 1)
                        nc.vector.tensor_copy(h_hi[:, c, :], h_sb[:, c, :]).then_inc(h_hi_ready, 1)
                elif before:
                    dve.wait_ge(stats_ready, TILES * g)
                if before:
                    for t in range(TILES):
                        nc.vector.bn_aggr(mean_var[:, t, :], stats[:, t, :]).then_inc(aggr_ready, 1)
                    dve.wait_ge(aggr_ready, TILES * g)
                    nc.vector.tensor_scalar(var_eps[:], mean_var[:, :, 1:2].rearrange("p t o -> p (t o)"), LN_EPS, None,
                                            ALU.add).then_inc(var_ready, 1)
                if before:
                    dve.wait_ge(rstd_ready, g)
                    if looped or g >= 3:
                        dve.wait_ge(stored[1 - p], 8 * (g - 1 - (1 - p)))
                    for t in range(TILES):
                        nc.vector.tensor_scalar(normed[1 - p][:, t, :], res[:, t, :], mean_var[:, t, 0:1],
                                                rstd[:, t:t + 1], ALU.subtract, ALU.mult).then_inc(norm_done, 1)
                if after:
                    row_part(g + 1)

            run_steps(dve, step)
            dve.wait_ge(type_max_ready, GROUPS)
            nc.vector.tensor_reduce(type_col[:], type_max[:], AX.XY, ALU.max).then_inc(type_max_ready, 1)
            dve.wait_ge(type_zeroed, 2)
            nc.vector.tensor_copy(type_ids[:], type_iota[:]).then_inc(type_max_ready, 1)
            dve.wait_ge(type_max_ready, GROUPS + 2)
            dve.wait_ge(type_all_ready, 1)
            nc.vector.tensor_copy(type_flag[:], type_all[:]).then_inc(type_flag_ready, 1)

            def typed_tile(g, q, n):
                def after(k, base):
                    dve.wait_ge(t_vec, base + k)

                front = T_ALL * n
                dve.wait_ge(t_front_done, n + 1)
                for c in range(KC):
                    nc.vector.tensor_copy(t_z[:, c, :], col_ps[c][:, 0:P]).then_inc(t_vec, 1)
                nc.vector.tensor_copy(t_y, row_ps[:, 0, 0:HID]).then_inc(t_vec, 1)
                nc.vector.tensor_tensor(t_row[:], row_ps[:, 1, 0:TYPES], c1c2[:], ALU.add).then_inc(t_vec, 1)
                nc.vector.tensor_copy(t_adj, adj_sb[:, bass.ds(g, 1), bass.ds(q, 1), :].rearrange("p a b n -> p (a b n)")).then_inc(t_vec, 1)
                nc.vector.memset(t_sum, 0.0).then_inc(t_vec, 1)
                dve.wait_ge(t_in, 32 * (n + 1))
                nc.vector.tensor_tensor(t_xb, t_x, wo_b_sb[:], ALU.add).then_inc(t_vec, 1)

                with dve.Fori(0, EDGE_TYPES) as e:
                    base = T_ALL * n + T_FRONT + T_TYPE * e
                    one = bass.ds(e + 1, 1)
                    after(0, base)
                    for c in range(KC):
                        nc.vector.tensor_scalar(t_zt[:, c, :], t_z[:, c, :], w2c1[:, c, one], None,
                                                ALU.add).then_inc(t_vec, 1)
                    dve.wait_ge(t_rel_done, EDGE_TYPES * n + e + 1)
                    for b in range(2):
                        r = slice(b * NODES, (b + 1) * NODES)
                        nc.vector.tensor_scalar(t_rel[r], att_ps[r, 0, r], t_row[r, one], None,
                                                ALU.add).then_inc(t_vec, 1)
                    after(KC + 2, base)
                    nc.vector.scalar_tensor_tensor(out=t_picked, in0=t_adj, scalar=type_ids[:, one], in1=t_rel,
                                                   op0=ALU.is_equal, op1=ALU.mult).then_inc(t_vec, 1)
                    after(KC + 3, base)
                    nc.vector.tensor_tensor(t_sum, t_sum, t_picked, ALU.add).then_inc(t_vec, 1)

                rest = T_ALL * n + T_FRONT + EDGE_TYPES * T_TYPE
                nc.vector.tensor_scalar(t_neg, t_adj, 0.0, NEG, ALU.is_equal, ALU.mult).then_inc(t_vec, 1)
                after(1, rest)
                nc.vector.tensor_tensor(t_masked, t_sum, t_neg, ALU.add).then_inc(t_vec, 1)
                after(2, rest)
                nc.vector.tensor_reduce(t_neg_max, t_masked, AX.X, ALU.max, negate=True).then_inc(t_vec, 1)
                dve.wait_ge(t_exp_done, n + 1)
                nc.vector.reciprocal(t_exp_inv, t_exp_sum).then_inc(t_vec, 1)
                after(4, rest)
                for b in range(2):
                    r = slice(b * NODES, (b + 1) * NODES)
                    nc.vector.tensor_scalar(attn[r, 0, r], t_exp[r], t_exp_inv[r], None, ALU.mult).then_inc(t_vec, 1)
                dve.wait_ge(t_attnT_done, n + 1)
                nc.vector.tensor_copy(t_attnT, att_ps[:, 1, :]).then_inc(t_vec, 1)
                dve.wait_ge(t_out_done, n + 1)
                nc.vector.tensor_tensor(t_res, row_ps[:, 0, 0:HID], t_xb, ALU.add).then_inc(t_vec, 1)
                after(8, rest)
                nc.vector.tensor_reduce(t_total, t_res, AX.X, ALU.add).then_inc(t_vec, 1)
                after(9, rest)
                nc.vector.tensor_scalar(t_mean, t_total, 1.0 / HID, None, ALU.mult).then_inc(t_vec, 1)
                after(10, rest)
                nc.vector.tensor_scalar(t_centred, t_res, t_mean, None, ALU.subtract).then_inc(t_vec, 1)
                after(11, rest)
                nc.vector.tensor_tensor(t_sq, t_centred, t_centred, ALU.mult).then_inc(t_vec, 1)
                after(12, rest)
                nc.vector.tensor_reduce(t_sqsum, t_sq, AX.X, ALU.add).then_inc(t_vec, 1)
                after(13, rest)
                nc.vector.tensor_scalar(t_var, t_sqsum, 1.0 / HID, LN_EPS, ALU.mult, ALU.add).then_inc(t_vec, 1)
                dve.wait_ge(t_rstd_ready, n + 1)
                nc.vector.tensor_scalar(t_out, t_centred, t_rstd, None, ALU.mult).then_inc(t_vec, 1)
                dve.wait_ge(t_stored, 16 * (n + 1))

            typed_pass(dve, typed_tile)

        @block.tensor
        def _(pe):
            def product(out_ap, hi_l, lo_l, hi_r, lo_r, first, last):
                nc.tensor.matmul(out_ap, hi_l, hi_r, start=first, stop=False)
                nc.tensor.matmul(out_ap, hi_l, lo_r, start=False, stop=False)
                return nc.tensor.matmul(out_ap, lo_l, hi_r, start=False, stop=last)

            pe.wait_ge(small_in, 48)
            for k in range(2):
                for c in range(KC):
                    nc.tensor.matmul(row_ps[:, k, c * TYPES:(c + 1) * TYPES], wdep_sb[:, k, c * P:(c + 1) * P],
                                     embT_sb[:], start=True, stop=True).then_inc(c_ps_done, 1)
            pe.wait_ge(w1_in, 16)
            pe.wait_ge(w2_in, 16)
            for c in range(KC):
                for e in range(KC):
                    mm = nc.tensor.matmul(col_ps[c][:, 0:HID], w1T_sb[:, e, c * P:(c + 1) * P], w2T_sb[:, e, :],
                                          start=(e == 0), stop=(e == KC - 1))
                mm.then_inc(m_ps_done, 1)
            pe.wait_ge(c_ready, 2 * KC + 1)
            for bank, w, table in ((2, w2T_sb, c1), (3, w1T_sb, c2)):
                for c in range(KC):
                    for e in range(KC):
                        mm = nc.tensor.matmul(row_ps[:, bank, c * TYPES:(c + 1) * TYPES], w[:, e, c * P:(c + 1) * P],
                                              table[:, e, :], start=(e == 0), stop=(e == KC - 1))
                mm.then_inc(table_ps_done, 1)
            pe.wait_ge(consts_ready, 2)
            for e in range(KC):
                mm = nc.tensor.matmul(row_ps[:, 0, 256:256 + TYPES], ones[:], c12[:, e, :],
                                      start=(e == 0), stop=(e == KC - 1))
            mm.then_inc(table_ps_done, 1)

            def z_chunk(p, c):
                o = slice(c * P, (c + 1) * P)
                for k in range(KC):
                    mm = product(col_ps[c][:], m_hi[:, k, o], m_lo[:, k, o], xT_hi[p][:, k, :], xT_lo[p][:, k, :],
                                 k == 0, k == KC - 1)
                mm.then_inc(z_done, 1)

            def y_tile(p, t):
                o = slice(t * P, (t + 1) * P)
                for k in range(KC):
                    mm = product(row_ps[:, t, 0:YW], xT_hi[p][:, k, o], xT_lo[p][:, k, o], gcn_hi[:, k, :],
                                 gcn_lo[:, k, :], k == 0, k == KC - 1)
                mm.then_inc(y_done, 1)

            def out_tile(t):
                o = slice(t * P, (t + 1) * P)
                for k in range(KC):
                    mm = product(row_ps[:, t, 0:HID], h_hi[:, k, o], h_lo[:, k, o], wo_hi[:, k, :], wo_lo[:, k, :],
                                 k == 0, k == KC - 1)
                mm.then_inc(out_done, 1)

            pe.wait_ge(w_split, 1)
            pe.wait_ge(x_lo_ready, KC)
            for c in range(KC):
                z_chunk(0, c)
            pe.wait_ge(gcn_split, 4)
            pe.wait_ge(table_ready, 3)
            for t in range(TILES):
                y_tile(0, t)

            def step(g, p, looped=False):
                live = looped or g < GROUPS
                before = looped or g >= 1
                after = looped or g + 1 < GROUPS
                if live:
                    pe.wait_ge(z_ready, KC * (g + 1))
                    if before:
                        pe.wait_ge(attnT_ready, g)
                    for t in range(TILES):
                        for b in range(2):
                            o = slice(t * P + b * NODES, t * P + (b + 1) * NODES)
                            for k in range(KC):
                                mm = nc.tensor.matmul(att_ps[b * NODES:(b + 1) * NODES, t, 0:NODES], z_sb[:, k, o],
                                                      xT_sb[p][:, k, o], start=(k == 0), stop=(k == KC - 1))
                    mm.then_inc(rel_done, 1)
                if after:
                    pe.wait_ge(x_lo_ready, KC * (g + 2))
                    for c in range(KC):
                        if before:
                            pe.wait_ge(relu_done, KC * (g - 1) + c + 1)
                        z_chunk(1 - p, c)
                if before:
                    if not looped and g == 1:
                        pe.wait_ge(wo_split, 2)
                    pe.wait_ge(h_lo_ready, KC * g)
                    if live:
                        pe.wait_ge(y_ready, TILES * (g + 1))
                    out_tile(0)
                    out_tile(1)
                if live:
                    if not looped and g == 0:
                        pe.wait_ge(consts_ready, 4)
                    pe.wait_ge(attn_ready, 2 * (g + 1))
                    for t in range(TILES):
                        mm = nc.tensor.transpose(att_ps[:, t, :], attn[:, t, :], ident[:])
                    mm.then_inc(attnT_done, 1)
                if before:
                    out_tile(2)
                    out_tile(3)
                if live:
                    pe.wait_ge(attnT_ready, g + 1)
                    for c in range(KC):
                        if after:
                            pe.wait_ge(z_ready, KC * (g + 1) + c + 1)
                        for t in range(TILES):
                            o = slice(t * P, (t + 1) * P)
                            mm = nc.tensor.matmul(col_ps[c][:, o], y_sb[:, t, c * P:(c + 1) * P], attnT[:, o],
                                                  start=True, stop=True)
                        mm.then_inc(h_done, 1)
                if after:
                    for t in range(TILES):
                        if before:
                            pe.wait_ge(res_ready, TILES * (g - 1) + t + 1)
                        y_tile(1 - p, t)

            run_steps(pe, step)

            def typed_tile(g, q, n):
                pe.wait_ge(t_in, 32 * (n + 1))
                for c in range(KC):
                    for k in range(KC):
                        nc.tensor.matmul(col_ps[c][:, 0:P], m_sb[:, k, c * P:(c + 1) * P], t_xT[:, k, :],
                                         start=(k == 0), stop=(k == KC - 1))
                for k in range(KC):
                    nc.tensor.matmul(row_ps[:, 0, 0:HID], t_xT[:, k, :], gcn_sb[:, k, 0:HID],
                                     start=(k == 0), stop=(k == KC - 1))
                for k in range(KC):
                    mm = nc.tensor.matmul(row_ps[:, 1, 0:TYPES], t_xT[:, k, :], w1c2[:, k, :],
                                          start=(k == 0), stop=(k == KC - 1))
                mm.then_inc(t_front_done, 1)
                with pe.Fori(0, EDGE_TYPES) as e:
                    pe.wait_ge(t_vec, T_ALL * n + T_FRONT + T_TYPE * e + KC)
                    for k in range(KC):
                        mm = nc.tensor.matmul(att_ps[:, 0, :], t_zt[:, k, :], t_xT[:, k, :],
                                              start=(k == 0), stop=(k == KC - 1))
                    mm.then_inc(t_rel_done, 1)
                rest = T_ALL * n + T_FRONT + EDGE_TYPES * T_TYPE
                pe.wait_ge(t_vec, rest + 6)
                nc.tensor.transpose(att_ps[:, 1, :], attn[:, 0, :], ident[:]).then_inc(t_attnT_done, 1)
                pe.wait_ge(t_vec, rest + 7)
                for c in range(KC):
                    mm = nc.tensor.matmul(col_ps[c][:, 0:P], t_y[:, c * P:(c + 1) * P], t_attnT, start=True, stop=True)
                mm.then_inc(t_h_done, 1)
                pe.wait_ge(t_relu_done, KC * (n + 1))
                for k in range(KC):
                    mm = nc.tensor.matmul(row_ps[:, 0, 0:HID], t_h[:, k, :], wo_sb[:, k, :],
                                          start=(k == 0), stop=(k == KC - 1))
                mm.then_inc(t_out_done, 1)

            typed_pass(pe, typed_tile)


def kernel(**inputs):
    import numpy as np
    import concourse.bacc as bacc
    from concourse import mybir as mb
    from concourse.bass_utils import run_bass_kernel_spmd

    pre = "L0_gnn_"
    x = np.asarray(inputs["x"])
    adj = np.asarray(inputs["adj"])
    graphs, nodes, hid = x.shape
    kc, tiles = hid // 128, 4
    tok = tiles * 128
    groups = graphs * nodes // tok
    w1, w2 = np.asarray(inputs[pre + "W1_w"]), np.asarray(inputs[pre + "W2_w"])

    def rows(w):
        return w.reshape(-1, 128, w.shape[1]).transpose(1, 0, 2)

    def cols(b):
        return b.reshape(-1, 128).T

    laid = {
        "xT": x.reshape(groups, tok, kc, 128).transpose(0, 3, 2, 1),
        "xn": x.reshape(groups, tiles, 128, hid).transpose(0, 2, 1, 3),
        "adj": adj.reshape(groups, tiles, 128, nodes).transpose(0, 2, 1, 3),
        "embT": np.asarray(inputs[pre + "dep_emb_table"]).T,
        "w1T": rows(w1[:hid].T),
        "w2T": rows(w2[:hid].T),
        "wdep": np.stack([w1[hid:], w2[hid:]], axis=1),
        "gcn_w": rows(np.asarray(inputs[pre + "gcn_w"])),
        "wo_w": rows(np.asarray(inputs[pre + "Wo_w"])),
        "bias_cols": np.stack([cols(np.asarray(inputs[pre + b])) for b in ("W1_b", "W2_b", "gcn_b")], axis=1),
        "wo_b": np.asarray(inputs[pre + "Wo_b"]),
    }
    nc = bacc.Bacc("TRN2", target_bir_lowering=False, num_devices=1)
    arrays, args = {}, []
    for name, a in laid.items():
        a = np.ascontiguousarray(a)
        arrays[f"in_{name}_dram"] = a
        args.append(nc.dram_tensor(f"in_{name}_dram", a.shape, mb.dt.from_np(a.dtype), kind="ExternalInput").ap())
    args.append(nc.dram_tensor("out_0_dram", (groups, 128, tiles, hid), mb.dt.float32, kind="ExternalOutput").ap())
    adj_resnorm_kernel(nc, *args)
    r = run_bass_kernel_spmd(nc, [arrays], core_ids=[0])
    got = r.results[0]["out_0_dram"]
    return got.reshape(groups, 128, tiles, hid).transpose(0, 2, 1, 3).reshape(graphs, nodes, hid)
```

```python
from contextlib import ExitStack

import concourse.bass as bass
from concourse import mybir

ALU = mybir.AluOpType
ACT = mybir.ActivationFunctionType
AX = mybir.AxisListType
F32 = mybir.dt.float32
F32R = mybir.dt.float32r
I32 = mybir.dt.int32

P = 128
NEG = -1000000000.0
LN_EPS = 1e-05


def adj_resnorm_kernel(
    nc: bass.Bass,
    xT: bass.AP,
    xn: bass.AP,
    adj: bass.AP,
    w1T: bass.AP,
    w2T: bass.AP,
    dep: bass.AP,
    gcn_w: bass.AP,
    wo_w: bass.AP,
    bias_cols: bass.AP,
    wo_b: bass.AP,
    out: bass.AP,
):
    GROUPS, _, KC, TOK = xT.shape
    HID = KC * P
    TILES = TOK // P
    NODES = adj.shape[3]
    DEP = dep.shape[0]
    TYPES = dep.shape[1] - 2 * HID
    YW = HID + 2

    ctx = ExitStack()
    with ctx:
        def sb(name, shape, dt=F32):
            return ctx.enter_context(nc.sbuf_tensor(name, shape, dt))

        def ps(name, shape):
            return ctx.enter_context(nc.psum_tensor(name, shape, F32))

        def sem(name):
            return ctx.enter_context(nc.semaphore(name))

        w1T_sb = sb("w1T_sb", [P, KC, HID])
        w2T_c2 = sb("w2T_c2", [P, KC, HID + TYPES])
        w2T_sb = w2T_c2[:, :, 0:HID]
        c2 = w2T_c2[:, :, HID:HID + TYPES]
        dep_sb = sb("dep_sb", [DEP, 2 * HID + TYPES])
        embT_sb = dep_sb[:, 2 * HID:2 * HID + TYPES]
        gcn_sb = sb("gcn_sb", [P, KC, YW])
        wo_sb = sb("wo_sb", [P, KC, HID])
        bias_sb = sb("bias_sb", [P, 3, KC])
        wo_b_sb = sb("wo_b_sb", [P, HID])
        ones = sb("ones", [P, P])
        ident = sb("ident", [P, P])
        minus_half = sb("minus_half", [P, TILES])
        c1 = sb("c1", [P, KC, TYPES])
        c12 = sb("c12", [P, KC, TYPES])
        w2c1 = sb("w2c1", [P, KC, TYPES])
        w1c2 = sb("w1c2", [P, KC, TYPES])
        c1c2 = sb("c1c2", [P, TYPES])
        m_sb = sb("m_sb", [P, KC, HID])
        m_hi = sb("m_hi", [P, KC, HID], F32R)
        m_lo = sb("m_lo", [P, KC, HID], F32R)
        gcn_hi = sb("gcn_hi", [P, KC, YW], F32R)
        gcn_lo = sb("gcn_lo", [P, KC, YW], F32R)
        wo_hi = sb("wo_hi", [P, KC, HID], F32R)
        wo_lo = sb("wo_lo", [P, KC, HID], F32R)
        adj_sb = sb("adj_sb", [P, GROUPS, TILES, NODES], I32)

        xT_sb = [sb(f"xT_sb{p}", [P, KC, TOK]) for p in range(2)]
        xT_hi = [sb(f"xT_hi{p}", [P, KC, TOK], F32R) for p in range(2)]
        xT_lo = [sb(f"xT_lo{p}", [P, KC, TOK], F32R) for p in range(2)]
        xb = [sb(f"xb{p}", [P, TILES, HID]) for p in range(2)]
        z_sb = sb("z_sb", [P, KC, TOK])
        y_sb = sb("y_sb", [P, TILES, YW])
        row_term = sb("row_term", [P, TILES])
        neg_mask = sb("neg_mask", [P, TILES, NODES])
        rel = sb("rel", [P, TILES, NODES])
        rel_kept = sb("rel_kept", [P, TILES, NODES])
        masked = sb("masked", [P, TILES, NODES])
        neg_max = sb("neg_max", [P, TILES])
        expd = sb("expd", [P, TILES, NODES])
        exp_sum = sb("exp_sum", [P, TILES])
        exp_inv = sb("exp_inv", [P, TILES])
        attn = sb("attn", [P, TILES, P])
        attnT = sb("attnT", [P, TOK])
        h_sb = sb("h_sb", [P, KC, TOK])
        h_hi = sb("h_hi", [P, KC, TOK], F32R)
        h_lo = sb("h_lo", [P, KC, TOK], F32R)
        res = sb("res", [P, TILES, HID])
        stats = sb("stats", [P, TILES, 6])
        mean_var = sb("mean_var", [P, TILES, 2])
        var_eps = sb("var_eps", [P, TILES])
        rstd = sb("rstd", [P, TILES])
        shift = sb("shift", [P, TILES])
        normed = [sb(f"normed{p}", [P, TILES, HID]) for p in range(2)]

        type_max = sb("type_max", [P, TILES, NODES], I32)
        type_col = sb("type_col", [P, 1])
        type_all = sb("type_all", [P, 1])
        type_flag = sb("type_flag", [P, 1], I32)
        type_ids = sb("type_ids", [P, TYPES])
        type_iota = sb("type_iota", [P, TYPES], I32)

        t_xT = xT_sb[0][:, :, 0:P]
        t_x = xb[0][:, 0, :]
        t_xb = xb[0][:, 1, :]
        t_out = normed[0][:, 0, :]
        t_sq = normed[0][:, 1, :]
        t_z = xT_sb[1][:, :, 0:P]
        t_zt = xT_sb[1][:, :, P:2 * P]
        t_h = xT_sb[1][:, :, 2 * P:3 * P]
        t_y = res[:, 1, :]
        t_res = res[:, 0, :]
        t_centred = res[:, 2, :]
        t_attnT = res[:, 3, 0:P]
        t_adj = rel[:, 0, :]
        t_rel = rel_kept[:, 0, :]
        t_picked = rel_kept[:, 1, :]
        t_sum = masked[:, 0, :]
        t_neg = masked[:, 1, :]
        t_masked = masked[:, 2, :]
        t_exp = expd[:, 0, :]
        t_row = sb("t_row", [P, TYPES])
        t_small = sb("t_small", [P, 8])
        t_neg_max, t_exp_sum, t_exp_inv, t_total, t_mean, t_sqsum, t_var, t_rstd = (
            t_small[:, k:k + 1] for k in range(8))

        att_ps = ps("att_ps", [P, TILES, P])
        col_ps = [ps(f"col_ps{c}", [P, TOK]) for c in range(KC)]
        row_ps = ps("row_ps", [P, TILES, 512])

        w1_in = [sem(f"w1_in{c}") for c in range(KC)]
        w2_in, dep_in, bias_in, gcn_in, wo_in, wo_b_in = (
            sem(n) for n in ("w2_in", "dep_in", "bias_in", "gcn_in", "wo_in", "wo_b_in"))
        adj_in = [sem(f"adj_in{k}") for k in range(2)]
        xT_in = [sem(f"xT_in{p}") for p in range(2)]
        xn_in = [sem(f"xn_in{p}") for p in range(2)]
        stored = [sem(f"stored{p}") for p in range(2)]
        consts_ready = sem("consts_ready")
        c_ps_done = sem("c_ps_done")
        c_ready = sem("c_ready")
        m_ps_done = sem("m_ps_done")
        m_hi_ready = sem("m_hi_ready")
        m_lo_ready = sem("m_lo_ready")
        w1c2_ready = sem("w1c2_ready")
        table_ps_done = sem("table_ps_done")
        table_ready = sem("table_ready")
        gcn_split, wo_split, attn_zeroed = sem("gcn_split"), sem("wo_split"), sem("attn_zeroed")
        x_hi_ready = sem("x_hi_ready")
        x_lo_ready = sem("x_lo_ready")
        xb_ready = sem("xb_ready")
        z_done = sem("z_done")
        z_ready = sem("z_ready")
        y_done = sem("y_done")
        y_ready = sem("y_ready")
        row_ready = sem("row_ready")
        rel_done = sem("rel_done")
        neg_mask_ready = sem("neg_mask_ready")
        soft_step = sem("soft_step")
        max_ready = sem("max_ready")
        exp_done = sem("exp_done")
        inv_ready = sem("inv_ready")
        attn_ready = sem("attn_ready")
        attnT_done = sem("attnT_done")
        attnT_ready = sem("attnT_ready")
        h_done = sem("h_done")
        relu_done = sem("relu_done")
        h_hi_ready = sem("h_hi_ready")
        h_lo_ready = sem("h_lo_ready")
        out_done = sem("out_done")
        res_ready = sem("res_ready")
        stats_ready = sem("stats_ready")
        aggr_ready = sem("aggr_ready")
        var_ready = sem("var_ready")
        rstd_ready = sem("rstd_ready")
        shift_ready = sem("shift_ready")
        norm_done = sem("norm_done")

        type_max_ready = sem("type_max_ready")
        type_all_ready = sem("type_all_ready")
        type_flag_ready = sem("type_flag_ready")
        type_zeroed = sem("type_zeroed")
        t_m_ready = sem("t_m_ready")
        t_in = sem("t_in")
        t_front_done = sem("t_front_done")
        t_rel_done = sem("t_rel_done")
        t_exp_done = sem("t_exp_done")
        t_attnT_done = sem("t_attnT_done")
        t_h_done = sem("t_h_done")
        t_relu_done = sem("t_relu_done")
        t_out_done = sem("t_out_done")
        t_rstd_ready = sem("t_rstd_ready")
        t_vec = sem("t_vec")
        t_stored = sem("t_stored")

        T_FRONT, T_TYPE, T_REST = KC + 5, KC + 4, 15
        EDGE_TYPES = TYPES - 1
        T_ALL = T_FRONT + EDGE_TYPES * T_TYPE + T_REST

        def typed_pass(eng, tile, first=None, stores=False):
            eng.wait_ge(type_flag_ready, 1)
            greatest = eng.value_load(type_flag[0:1, 0:1], min_val=0, max_val=TYPES - 1)
            if stores:
                q = (GROUPS - 1) % 2
                eng.wait_ge(stored[1 - q], 16 * (GROUPS // 2))
                eng.wait_ge(stored[q], 16 * (GROUPS // 2 - 1 + TILES))
            with eng.If(greatest > 1):
                if first:
                    first()
                with eng.Fori(0, GROUPS) as g:
                    with eng.Fori(0, TILES) as q:
                        tile(g, q, TILES * g + q)
                if stores:
                    eng.wait_ge(t_stored, 16 * GROUPS * TILES)

        LAST_LOTS = ((0, 1), (2,), (3,))

        FIRST_LOOPED, LAST_LOOPED = 3, GROUPS - 4

        def run_steps(eng, step):
            for g in range(FIRST_LOOPED):
                step(g, g % 2)
            with eng.Fori(0, (LAST_LOOPED - FIRST_LOOPED + 1) // 2) as i:
                for g in range(FIRST_LOOPED, FIRST_LOOPED + 2):
                    step(2 * i + g, g % 2, True)
            for g in range(LAST_LOOPED + 1, GROUPS + 1):
                step(g, g % 2)

        block = ctx.enter_context(nc.Block())

        @block.sync
        def _(sp):
            sp.dma_start(dep_sb[:], dep).then_inc(dep_in, 16)
            sp.dma_start(w2T_sb, w2T).then_inc(w2_in, 16)
            sp.dma_start(xT_sb[0][:], xT[0]).then_inc(xT_in[0], 16)
            sp.dma_start(xT_sb[1][:], xT[1]).then_inc(xT_in[1], 16)
            for k, some in enumerate((slice(0, FIRST_LOOPED), slice(FIRST_LOOPED, GROUPS))):
                sp.dma_start(adj_sb[:, some].rearrange("p g t n -> p g (t n)"),
                             adj[some].rearrange("g p t n -> p g (t n)")).then_inc(adj_in[k], 16)
                sp.dma_start(xb[k][:], xn[k]).then_inc(xn_in[k], 16)

            def step(g, p, looped=False):
                if looped or g + 2 < GROUPS:
                    sp.wait_ge(rel_done, g + 1)
                    sp.dma_start(xT_sb[p][:], xT[g + 2]).then_inc(xT_in[p], 16)
                if looped or 1 <= g <= GROUPS - 2:
                    sp.wait_ge(res_ready, TILES * g)
                    sp.dma_start(xb[1 - p][:], xn[g + 1]).then_inc(xn_in[1 - p], 16)
                if looped or 1 <= g < GROUPS:
                    sp.wait_ge(norm_done, TILES * g)
                    sp.dma_start(out[g - 1], normed[1 - p][:]).then_inc(stored[1 - p], 16)

            run_steps(sp, step)
            q = (GROUPS - 1) % 2
            for t in range(TILES):
                sp.wait_ge(norm_done, TILES * (GROUPS - 1) + t + 1)
                sp.dma_start(out[GROUPS - 1, :, t, :], normed[q][:, t, :]).then_inc(stored[q], 16)

            def typed_tile(g, q, n):
                sp.dma_start(t_xT, xT[g, :, :, bass.ds(q * P, P)]).then_inc(t_in, 16)
                sp.dma_start(t_x, xn[g, :, bass.ds(q, 1), :].rearrange("p o d -> p (o d)")).then_inc(t_in, 16)
                sp.wait_ge(t_vec, T_ALL * (n + 1))
                sp.dma_start(out[g, :, bass.ds(q, 1), :].rearrange("p o d -> p (o d)"), t_out).then_inc(t_stored, 16)

            typed_pass(sp, typed_tile, stores=True)

        @block.gpsimd
        def _(pool):
            nc.gpsimd.memset(ident[:], 0.0).then_inc(consts_ready, 1)
            nc.gpsimd.memset(ones[:], 1.0).then_inc(consts_ready, 1)
            nc.gpsimd.memset(minus_half[:], -0.5).then_inc(consts_ready, 1)
            pool.wait_ge(consts_ready, 1)
            nc.gpsimd.affine_select(out=ident[:], in_=ident[:], compare_op=ALU.not_equal, fill=1.0, base=0,
                                    pattern=[[-1, P]], channel_multiplier=1).then_inc(consts_ready, 1)
            nc.gpsimd.memset(attn[:], 0.0).then_inc(attn_zeroed, 1)
            nc.gpsimd.memset(type_max[:], 0).then_inc(type_zeroed, 1)
            nc.gpsimd.iota(type_iota[:], pattern=[[1, TYPES]], base=0, channel_multiplier=0).then_inc(type_zeroed, 1)
            def x_lo_part(g, p):
                for c in range(KC):
                    pool.wait_ge(x_hi_ready, KC * g + c + 1)
                    nc.gpsimd.tensor_tensor(xT_lo[p][:, c, :], xT_sb[p][:, c, :], xT_hi[p][:, c, :].bitcast(F32),
                                            ALU.subtract).then_inc(x_lo_ready, 1)

            x_lo_part(1, 1)

            def step(g, p, looped=False):
                live = looped or g < GROUPS
                if live:
                    if not looped and g == 0:
                        pool.wait_ge(wo_b_in, 16)
                    pool.wait_ge(xn_in[p], 8 * (g - p) + 16)
                    for t in range(TILES):
                        nc.gpsimd.tensor_tensor(xb[p][:, t, :], xb[p][:, t, :], wo_b_sb[:], ALU.add).then_inc(xb_ready, 1)
                if looped or g + 2 < GROUPS:
                    x_lo_part(g + 2, p)
                if looped or g >= 1:
                    if not looped and g == 1:
                        pool.wait_ge(consts_ready, 3)
                    if live:
                        pool.wait_ge(var_ready, g)
                        nc.gpsimd.tensor_tensor(rstd[:], var_eps[:], minus_half[:], ALU.pow).then_inc(rstd_ready, 1)
                    else:
                        for n, lot in enumerate(LAST_LOTS):
                            o = slice(lot[0], lot[-1] + 1)
                            pool.wait_ge(var_ready, g + n)
                            nc.gpsimd.tensor_tensor(rstd[:, o], var_eps[:, o], minus_half[:, o],
                                                    ALU.pow).then_inc(rstd_ready, 1)
                if not looped and g == GROUPS - 1:
                    pool.wait_ge(type_max_ready, GROUPS + 1)
                    nc.gpsimd.partition_all_reduce(type_all[:], type_col[:], P,
                                                   bass.bass_isa.ReduceOp.max).then_inc(type_all_ready, 1)
                if looped or g < GROUPS - 1:
                    for c in range(KC):
                        pool.wait_ge(h_hi_ready, KC * g + c + 1)
                        nc.gpsimd.tensor_tensor(h_lo[:, c, :], h_sb[:, c, :], h_hi[:, c, :].bitcast(F32),
                                                ALU.subtract).then_inc(h_lo_ready, 1)

            run_steps(pool, step)

            def typed_tile(g, q, n):
                pool.wait_ge(t_vec, T_ALL * (n + 1) - 1)
                nc.gpsimd.tensor_tensor(t_rstd, t_var, minus_half[:, 0:1], ALU.pow).then_inc(t_rstd_ready, 1)

            typed_pass(pool, typed_tile)

        @block.scalar
        def _(act):
            act.dma_start(bias_sb[:], bias_cols).then_inc(bias_in, 16)
            for c in range(KC):
                o = slice(c * P, (c + 1) * P)
                act.dma_start(w1T_sb[:, :, o], w1T[:, :, o]).then_inc(w1_in[c], 16)
            act.dma_start(gcn_sb[:, :, 0:HID], gcn_w).then_inc(gcn_in, 16)
            act.dma_start(wo_sb[:], wo_w).then_inc(wo_in, 16)
            act.dma_start(wo_b_sb[:], wo_b.partition_broadcast(P)).then_inc(wo_b_in, 16)
            for c in range(KC):
                act.wait_ge(m_ps_done, c + 1)
                nc.scalar.activation(m_hi[:, c, :], col_ps[c][:, 0:HID], ACT.Identity).then_inc(m_hi_ready, 1)

            def z_part(g):
                for c in range(KC):
                    act.wait_ge(z_done, KC * g + c + 1)
                    nc.scalar.activation(z_sb[:, c, :], col_ps[c][:], ACT.Identity,
                                         bias=w2c1[:, c, 1:2]).then_inc(z_ready, 1)

            def y_part(g):
                for t in range(TILES):
                    act.wait_ge(y_done, TILES * g + t + 1)
                    nc.scalar.activation(y_sb[:, t, :], row_ps[:, t, 0:YW], ACT.Identity).then_inc(y_ready, 1)

            def neg_mask_part(g):
                if not isinstance(g, int) or g >= FIRST_LOOPED:
                    act.wait_ge(adj_in[1], 16)
                nc.scalar.activation(neg_mask[:], adj_sb[:, g], ACT.Copy, scale=-NEG,
                                     bias=NEG).then_inc(neg_mask_ready, 1)

            act.wait_ge(table_ready, 1)
            z_part(0)
            y_part(0)
            act.wait_ge(adj_in[0], 16)
            neg_mask_part(0)

            def norm_tile(q, t):
                nc.scalar.activation(normed[q][:, t, :], res[:, t, :], ACT.Identity, bias=shift[:, t:t + 1],
                                     scale=rstd[:, t:t + 1]).then_inc(norm_done, 1)

            def step(g, p, looped=False):
                if not looped and g == GROUPS:
                    act.wait_ge(stored[1 - p], 16 * (GROUPS // 2 - 1))
                    for n, lot in enumerate(LAST_LOTS):
                        act.wait_ge(shift_ready, GROUPS + n)
                        for t in lot:
                            norm_tile(1 - p, t)
                    return
                for t in range(TILES):
                    if t == 0:
                        act.wait_ge(max_ready, g + 1)
                    nc.scalar.activation(expd[:, t, :], masked[:, t, :], ACT.Exp, bias=neg_max[:, t:t + 1],
                                         accum_out=exp_sum[:, t:t + 1]).then_inc(exp_done, 1)
                if looped or g + 1 < GROUPS:
                    neg_mask_part(g + 1)
                    act.wait_ge(rel_done, g + 1)
                    z_part(g + 1)
                act.wait_ge(attnT_done, g + 1)
                if looped or g >= 1:
                    act.wait_ge(h_done, KC * g)
                nc.scalar.activation(attnT[:], att_ps[:].rearrange("p t n -> p (t n)"),
                                     ACT.Identity).then_inc(attnT_ready, 1)
                for c in range(KC):
                    if looped or g >= 1:
                        act.wait_ge(h_lo_ready, KC * (g - 1) + c + 1)
                    act.wait_ge(h_done, KC * g + c + 1)
                    nc.scalar.activation(h_sb[:, c, :], col_ps[c][:], ACT.Relu,
                                         bias=bias_sb[:, 2, c:c + 1]).then_inc(relu_done, 1)
                if looped or g + 1 < GROUPS:
                    y_part(g + 1)
                if looped or g >= 1:
                    act.wait_ge(shift_ready, g)
                    if looped or g >= 3:
                        act.wait_ge(stored[1 - p], 8 * (g - 1 - (1 - p)))
                    for t in range(TILES):
                        norm_tile(1 - p, t)

            run_steps(act, step)

            def typed_tile(g, q, n):
                at_rest = T_ALL * n + T_FRONT + EDGE_TYPES * T_TYPE
                act.wait_ge(t_vec, at_rest + 3)
                nc.scalar.activation(t_exp, t_masked, ACT.Exp, bias=t_neg_max,
                                     accum_out=t_exp_sum).then_inc(t_exp_done, 1)
                act.wait_ge(t_h_done, n + 1)
                for c in range(KC):
                    nc.scalar.activation(t_h[:, c, :], col_ps[c][:, 0:P], ACT.Relu,
                                         bias=bias_sb[:, 2, c:c + 1]).then_inc(t_relu_done, 1)

            typed_pass(act, typed_tile)

        @block.vector
        def _(dve):
            def x_hi_chunk(p, c):
                nc.vector.tensor_copy(xT_hi[p][:, c, :], xT_sb[p][:, c, :]).then_inc(x_hi_ready, 1)

            dve.wait_ge(bias_in, 16)
            dve.wait_ge(c_ps_done, 2 * KC)
            for k, table in ((1, c2), (0, c1[:])):
                for c in range(KC):
                    nc.vector.tensor_scalar(table[:, c, :], row_ps[:, k, c * TYPES:(c + 1) * TYPES],
                                            bias_sb[:, k, c:c + 1], None, ALU.add).then_inc(c_ready, 1)
            dve.wait_ge(c_ready, 2 * KC)
            nc.vector.tensor_tensor(c12[:], c1[:], c2, ALU.mult).then_inc(c_ready, 1)
            dve.wait_ge(xT_in[0], 16)
            for c in range(KC):
                x_hi_chunk(0, c)
                dve.wait_ge(x_hi_ready, c + 1)
                nc.vector.tensor_tensor(xT_lo[0][:, c, :], xT_sb[0][:, c, :], xT_hi[0][:, c, :].bitcast(F32),
                                        ALU.subtract).then_inc(x_lo_ready, 1)
            for c in range(KC):
                dve.wait_ge(m_hi_ready, c + 1)
                nc.vector.tensor_tensor(m_lo[:, c, :], col_ps[c][:, 0:HID], m_hi[:, c, :].bitcast(F32),
                                        ALU.subtract).then_inc(m_lo_ready, 1)
                nc.vector.tensor_copy(w1c2[:, c, :], col_ps[c][:, HID:HID + TYPES]).then_inc(w1c2_ready, 1)
            dve.wait_ge(table_ps_done, 2)
            nc.vector.tensor_copy(w2c1[:].rearrange("p c n -> p (c n)"), row_ps[:, 2, 0:KC * TYPES]).then_inc(table_ready, 1)
            nc.vector.tensor_copy(c1c2[:], row_ps[:, 2, KC * TYPES:(KC + 1) * TYPES]).then_inc(table_ready, 1)
            dve.wait_ge(gcn_in, 16)
            dve.wait_ge(w1c2_ready, KC)
            nc.vector.tensor_copy(gcn_sb[:, :, HID:HID + 1], w1c2[:, :, 1:2]).then_inc(gcn_split, 1)
            nc.vector.memset(gcn_sb[:, :, HID + 1:YW], 0.0).then_inc(gcn_split, 1)
            dve.wait_ge(gcn_split, 2)
            nc.vector.tensor_copy(gcn_hi[:], gcn_sb[:]).then_inc(gcn_split, 1)
            dve.wait_ge(gcn_split, 3)
            nc.vector.tensor_tensor(gcn_lo[:], gcn_sb[:], gcn_hi[:].bitcast(F32), ALU.subtract).then_inc(gcn_split, 1)
            dve.wait_ge(xT_in[1], 16)
            for c in range(KC):
                x_hi_chunk(1, c)
            dve.wait_ge(wo_in, 16)
            nc.vector.tensor_copy(wo_hi[:], wo_sb[:]).then_inc(wo_split, 1)
            dve.wait_ge(wo_split, 1)
            nc.vector.tensor_tensor(wo_lo[:], wo_sb[:], wo_hi[:].bitcast(F32), ALU.subtract).then_inc(wo_split, 1)

            def row_part(g):
                dve.wait_ge(y_ready, TILES * (g + 1))
                nc.vector.tensor_scalar(row_term[:], y_sb[:, :, HID:HID + 1].rearrange("p t o -> p (t o)"),
                                        c1c2[:, 1:2], None, ALU.add).then_inc(row_ready, 1)

            row_part(0)
            dve.wait_ge(attn_zeroed, 1)
            dve.wait_ge(type_zeroed, 1)

            def add_residual(q, t):
                nc.vector.tensor_tensor(res[:, t, :], row_ps[:, t, 0:HID], xb[q][:, t, :], ALU.add).then_inc(res_ready, 1)

            def residual(g, q, t):
                dve.wait_ge(out_done, TILES * g + t + 1)
                add_residual(q, t)
                dve.wait_ge(res_ready, TILES * g + t + 1)
                nc.vector.bn_stats(stats[:, t, :], res[:, t, :]).then_inc(stats_ready, 1)

            def type_partition_max():
                dve.wait_ge(type_max_ready, GROUPS)
                nc.vector.tensor_reduce(type_col[:], type_max[:], AX.XY, ALU.max).then_inc(type_max_ready, 1)
                dve.wait_ge(type_zeroed, 2)
                nc.vector.tensor_copy(type_ids[:], type_iota[:]).then_inc(type_max_ready, 1)

            def type_flag_part():
                dve.wait_ge(type_all_ready, 1)
                nc.vector.tensor_copy(type_flag[:], type_all[:]).then_inc(type_flag_ready, 1)

            def last_tiles():
                g, q = GROUPS - 1, (GROUPS - 1) % 2
                dve.wait_ge(xb_ready, TILES * GROUPS)
                for n, lot in enumerate(LAST_LOTS):
                    for t in lot:
                        dve.wait_ge(norm_done, TILES * (g - 1) + t + 1)
                        dve.wait_ge(out_done, TILES * g + t + 1)
                        add_residual(q, t)
                    for t in lot:
                        dve.wait_ge(res_ready, TILES * g + t + 1)
                        nc.vector.bn_stats(stats[:, t, :], res[:, t, :]).then_inc(stats_ready, 1)
                    if n == 0:
                        type_flag_part()
                    else:
                        shift_lot(n - 1)
                    dve.wait_ge(stats_ready, TILES * g + lot[-1] + 1)
                    for t in lot:
                        nc.vector.bn_aggr(mean_var[:, t, :], stats[:, t, :]).then_inc(aggr_ready, 1)
                    dve.wait_ge(aggr_ready, TILES * g + lot[-1] + 1)
                    nc.vector.tensor_scalar(var_eps[:, lot[0]:lot[-1] + 1],
                                            mean_var[:, lot[0]:lot[-1] + 1, 1:2].rearrange("p t o -> p (t o)"),
                                            LN_EPS, None, ALU.add).then_inc(var_ready, 1)
                shift_lot(n)

            def shift_lot(n):
                lot = LAST_LOTS[n]
                o = slice(lot[0], lot[-1] + 1)
                dve.wait_ge(rstd_ready, GROUPS + n)
                nc.vector.scalar_tensor_tensor(out=shift[:, o], in0=mean_var[:, o, 0:1].rearrange("p t o -> p (t o)"),
                                               scalar=-1.0, in1=rstd[:, o], op0=ALU.mult,
                                               op1=ALU.mult).then_inc(shift_ready, 1)

            def variance_part(g):
                for t in range(TILES):
                    nc.vector.bn_aggr(mean_var[:, t, :], stats[:, t, :]).then_inc(aggr_ready, 1)
                dve.wait_ge(aggr_ready, TILES * g)
                nc.vector.tensor_scalar(var_eps[:], mean_var[:, :, 1:2].rearrange("p t o -> p (t o)"), LN_EPS, None,
                                        ALU.add).then_inc(var_ready, 1)

            def shift_part(g):
                dve.wait_ge(rstd_ready, g)
                nc.vector.scalar_tensor_tensor(out=shift[:], in0=mean_var[:, :, 0:1].rearrange("p t o -> p (t o)"),
                                               scalar=-1.0, in1=rstd[:], op0=ALU.mult,
                                               op1=ALU.mult).then_inc(shift_ready, 1)

            def step(g, p, looped=False):
                live = looped or g < GROUPS
                last = not looped and g == GROUPS - 1
                before = looped or g >= 1
                after = looped or g + 1 < GROUPS
                if not live:
                    last_tiles()
                    return
                if live:
                    dve.wait_ge(row_ready, g + 1)
                    dve.wait_ge(rel_done, g + 1)
                    nc.vector.tensor_tensor(rel[:], att_ps[:, :, 0:NODES],
                                            row_term[:].rearrange("p (t o) -> p t o", o=1).to_broadcast([P, TILES, NODES]),
                                            ALU.add).then_inc(soft_step, 1)
                    dve.wait_ge(neg_mask_ready, g + 1)
                    dve.wait_ge(soft_step, 3 * g + 1)
                    nc.vector.tensor_tensor(rel_kept[:], rel[:], adj_sb[:, g], ALU.mult).then_inc(soft_step, 1)
                    if before:
                        dve.wait_ge(type_max_ready, g)
                    nc.vector.tensor_tensor(type_max[:], type_max[:], adj_sb[:, g], ALU.max).then_inc(type_max_ready, 1)
                    dve.wait_ge(soft_step, 3 * g + 2)
                    nc.vector.tensor_tensor(masked[:], rel_kept[:], neg_mask[:], ALU.add).then_inc(soft_step, 1)
                    dve.wait_ge(soft_step, 3 * g + 3)
                    nc.vector.tensor_reduce(neg_max[:], masked[:], AX.X, ALU.max, negate=True).then_inc(max_ready, 1)
                if not looped and g == GROUPS - 1:
                    type_partition_max()
                if live:
                    dve.wait_ge(exp_done, TILES * (g + 1))
                    nc.vector.reciprocal(exp_inv[:], exp_sum[:]).then_inc(inv_ready, 1)
                    dve.wait_ge(inv_ready, g + 1)
                    if before:
                        dve.wait_ge(attnT_done, g)
                    for b in range(2):
                        r = slice(b * NODES, (b + 1) * NODES)
                        nc.vector.tensor_tensor(attn[r, :, r], expd[r],
                                                exp_inv[r].rearrange("p (t o) -> p t o", o=1).to_broadcast([NODES, TILES, NODES]),
                                                ALU.mult).then_inc(attn_ready, 1)
                if before:
                    dve.wait_ge(xb_ready, TILES * g)
                    if looped or g >= 2:
                        dve.wait_ge(norm_done, TILES * (g - 1))
                    residual(g - 1, 1 - p, 0)
                    residual(g - 1, 1 - p, 1)
                if looped or g + 2 < GROUPS:
                    dve.wait_ge(xT_in[p], 8 * (g - p) + 32)
                    for c in range(KC):
                        x_hi_chunk(p, c)
                if before:
                    residual(g - 1, 1 - p, 2)
                    residual(g - 1, 1 - p, 3)
                if last:
                    dve.wait_ge(stats_ready, TILES * g)
                    variance_part(g)
                if live:
                    for c in range(KC):
                        if c == 0 and before:
                            dve.wait_ge(out_done, TILES * g)
                            dve.wait_ge(stats_ready, TILES * g)
                        dve.wait_ge(relu_done, KC * g + c + 1)
                        nc.vector.tensor_copy(h_hi[:, c, :], h_sb[:, c, :]).then_inc(h_hi_ready, 1)
                        if not looped and g == GROUPS - 1:
                            dve.wait_ge(h_hi_ready, KC * g + c + 1)
                            nc.vector.tensor_tensor(h_lo[:, c, :], h_sb[:, c, :], h_hi[:, c, :].bitcast(F32),
                                                    ALU.subtract).then_inc(h_lo_ready, 1)
                            if c == 1:
                                shift_part(g)
                if before and not last:
                    variance_part(g)
                    shift_part(g)
                if after:
                    row_part(g + 1)

            run_steps(dve, step)
            def typed_tile(g, q, n):
                def after(k, base):
                    dve.wait_ge(t_vec, base + k)

                front = T_ALL * n
                dve.wait_ge(t_front_done, n + 1)
                for c in range(KC):
                    nc.vector.tensor_copy(t_z[:, c, :], col_ps[c][:, 0:P]).then_inc(t_vec, 1)
                nc.vector.tensor_copy(t_y, row_ps[:, 0, 0:HID]).then_inc(t_vec, 1)
                nc.vector.tensor_tensor(t_row[:], row_ps[:, 1, 0:TYPES], c1c2[:], ALU.add).then_inc(t_vec, 1)
                nc.vector.tensor_copy(t_adj, adj_sb[:, bass.ds(g, 1), bass.ds(q, 1), :].rearrange("p a b n -> p (a b n)")).then_inc(t_vec, 1)
                nc.vector.memset(t_sum, 0.0).then_inc(t_vec, 1)
                dve.wait_ge(t_in, 32 * (n + 1))
                nc.vector.tensor_tensor(t_xb, t_x, wo_b_sb[:], ALU.add).then_inc(t_vec, 1)

                with dve.Fori(0, EDGE_TYPES) as e:
                    base = T_ALL * n + T_FRONT + T_TYPE * e
                    one = bass.ds(e + 1, 1)
                    after(0, base)
                    for c in range(KC):
                        nc.vector.tensor_scalar(t_zt[:, c, :], t_z[:, c, :], w2c1[:, c, one], None,
                                                ALU.add).then_inc(t_vec, 1)
                    dve.wait_ge(t_rel_done, EDGE_TYPES * n + e + 1)
                    for b in range(2):
                        r = slice(b * NODES, (b + 1) * NODES)
                        nc.vector.tensor_scalar(t_rel[r], att_ps[r, 0, r], t_row[r, one], None,
                                                ALU.add).then_inc(t_vec, 1)
                    after(KC + 2, base)
                    nc.vector.scalar_tensor_tensor(out=t_picked, in0=t_adj, scalar=type_ids[:, one], in1=t_rel,
                                                   op0=ALU.is_equal, op1=ALU.mult).then_inc(t_vec, 1)
                    after(KC + 3, base)
                    nc.vector.tensor_tensor(t_sum, t_sum, t_picked, ALU.add).then_inc(t_vec, 1)

                rest = T_ALL * n + T_FRONT + EDGE_TYPES * T_TYPE
                nc.vector.tensor_scalar(t_neg, t_adj, 0.0, NEG, ALU.is_equal, ALU.mult).then_inc(t_vec, 1)
                after(1, rest)
                nc.vector.tensor_tensor(t_masked, t_sum, t_neg, ALU.add).then_inc(t_vec, 1)
                after(2, rest)
                nc.vector.tensor_reduce(t_neg_max, t_masked, AX.X, ALU.max, negate=True).then_inc(t_vec, 1)
                dve.wait_ge(t_exp_done, n + 1)
                nc.vector.reciprocal(t_exp_inv, t_exp_sum).then_inc(t_vec, 1)
                after(4, rest)
                for b in range(2):
                    r = slice(b * NODES, (b + 1) * NODES)
                    nc.vector.tensor_scalar(attn[r, 0, r], t_exp[r], t_exp_inv[r], None, ALU.mult).then_inc(t_vec, 1)
                dve.wait_ge(t_attnT_done, n + 1)
                nc.vector.tensor_copy(t_attnT, att_ps[:, 1, :]).then_inc(t_vec, 1)
                dve.wait_ge(t_out_done, n + 1)
                nc.vector.tensor_tensor(t_res, row_ps[:, 0, 0:HID], t_xb, ALU.add).then_inc(t_vec, 1)
                after(8, rest)
                nc.vector.tensor_reduce(t_total, t_res, AX.X, ALU.add).then_inc(t_vec, 1)
                after(9, rest)
                nc.vector.tensor_scalar(t_mean, t_total, 1.0 / HID, None, ALU.mult).then_inc(t_vec, 1)
                after(10, rest)
                nc.vector.tensor_scalar(t_centred, t_res, t_mean, None, ALU.subtract).then_inc(t_vec, 1)
                after(11, rest)
                nc.vector.tensor_tensor(t_sq, t_centred, t_centred, ALU.mult).then_inc(t_vec, 1)
                after(12, rest)
                nc.vector.tensor_reduce(t_sqsum, t_sq, AX.X, ALU.add).then_inc(t_vec, 1)
                after(13, rest)
                nc.vector.tensor_scalar(t_var, t_sqsum, 1.0 / HID, LN_EPS, ALU.mult, ALU.add).then_inc(t_vec, 1)
                dve.wait_ge(t_rstd_ready, n + 1)
                nc.vector.tensor_scalar(t_out, t_centred, t_rstd, None, ALU.mult).then_inc(t_vec, 1)
                dve.wait_ge(t_stored, 16 * (n + 1))

            def typed_first():
                dve.wait_ge(type_max_ready, GROUPS + 2)
                nc.vector.tensor_tensor(m_sb[:], m_hi[:].bitcast(F32), m_lo[:].bitcast(F32), ALU.add).then_inc(t_m_ready, 1)

            typed_pass(dve, typed_tile, typed_first)

        @block.tensor
        def _(pe):
            def product(out_ap, hi_l, lo_l, hi_r, lo_r, first, last):
                nc.tensor.matmul(out_ap, hi_l, hi_r, start=first, stop=False)
                nc.tensor.matmul(out_ap, hi_l, lo_r, start=False, stop=False)
                return nc.tensor.matmul(out_ap, lo_l, hi_r, start=False, stop=last)

            pe.wait_ge(dep_in, 16)
            for k in range(2):
                for c in range(KC):
                    o = k * HID + c * P
                    nc.tensor.matmul(row_ps[:, k, c * TYPES:(c + 1) * TYPES], dep_sb[:, o:o + P], embT_sb,
                                     start=True, stop=True).then_inc(c_ps_done, 1)
            pe.wait_ge(w2_in, 16)
            pe.wait_ge(c_ready, KC)
            for c in range(KC):
                pe.wait_ge(w1_in[c], 16)
                for e in range(KC):
                    mm = nc.tensor.matmul(col_ps[c][:, 0:HID + TYPES], w1T_sb[:, e, c * P:(c + 1) * P], w2T_c2[:, e, :],
                                          start=(e == 0), stop=(e == KC - 1))
                mm.then_inc(m_ps_done, 1)
            pe.wait_ge(c_ready, 2 * KC + 1)
            for c in range(KC):
                for e in range(KC):
                    mm = nc.tensor.matmul(row_ps[:, 2, c * TYPES:(c + 1) * TYPES], w2T_sb[:, e, c * P:(c + 1) * P],
                                          c1[:, e, :], start=(e == 0), stop=(e == KC - 1))
            mm.then_inc(table_ps_done, 1)
            pe.wait_ge(consts_ready, 2)
            for e in range(KC):
                mm = nc.tensor.matmul(row_ps[:, 2, KC * TYPES:(KC + 1) * TYPES], ones[:], c12[:, e, :],
                                      start=(e == 0), stop=(e == KC - 1))
            mm.then_inc(table_ps_done, 1)

            def z_chunk(p, c):
                o = slice(c * P, (c + 1) * P)
                for k in range(KC):
                    mm = product(col_ps[c][:], m_hi[:, k, o], m_lo[:, k, o], xT_hi[p][:, k, :], xT_lo[p][:, k, :],
                                 k == 0, k == KC - 1)
                mm.then_inc(z_done, 1)

            def y_tile(p, t):
                o = slice(t * P, (t + 1) * P)
                for k in range(KC):
                    mm = product(row_ps[:, t, 0:YW], xT_hi[p][:, k, o], xT_lo[p][:, k, o], gcn_hi[:, k, :],
                                 gcn_lo[:, k, :], k == 0, k == KC - 1)
                mm.then_inc(y_done, 1)

            def out_tiles_by_chunk(tiles):
                for k in range(KC):
                    pe.wait_ge(h_lo_ready, KC * (GROUPS - 1) + k + 1)
                    for t in tiles:
                        o = slice(t * P, (t + 1) * P)
                        pe.wait_ge(res_ready, TILES * (GROUPS - 2) + t + 1)
                        mm = product(row_ps[:, t, 0:HID], h_hi[:, k, o], h_lo[:, k, o], wo_hi[:, k, :], wo_lo[:, k, :],
                                     k == 0, k == KC - 1)
                        if k == KC - 1:
                            mm.then_inc(out_done, 1)

            def out_tile(t):
                o = slice(t * P, (t + 1) * P)
                for k in range(KC):
                    mm = product(row_ps[:, t, 0:HID], h_hi[:, k, o], h_lo[:, k, o], wo_hi[:, k, :], wo_lo[:, k, :],
                                 k == 0, k == KC - 1)
                mm.then_inc(out_done, 1)

            pe.wait_ge(m_lo_ready, KC)
            pe.wait_ge(w1c2_ready, KC)
            pe.wait_ge(x_lo_ready, KC)
            for c in range(KC):
                z_chunk(0, c)
            pe.wait_ge(gcn_split, 4)
            pe.wait_ge(table_ready, 2)
            for t in range(TILES):
                y_tile(0, t)

            def step(g, p, looped=False):
                live = looped or g < GROUPS
                before = looped or g >= 1
                after = looped or g + 1 < GROUPS
                if live:
                    pe.wait_ge(z_ready, KC * (g + 1))
                    if before:
                        pe.wait_ge(attnT_ready, g)
                    for t in range(TILES):
                        for b in range(2):
                            o = slice(t * P + b * NODES, t * P + (b + 1) * NODES)
                            for k in range(KC):
                                mm = nc.tensor.matmul(att_ps[b * NODES:(b + 1) * NODES, t, 0:NODES], z_sb[:, k, o],
                                                      xT_sb[p][:, k, o], start=(k == 0), stop=(k == KC - 1))
                    mm.then_inc(rel_done, 1)
                if after:
                    pe.wait_ge(x_lo_ready, KC * (g + 2))
                    for c in range(KC):
                        if before:
                            pe.wait_ge(relu_done, KC * (g - 1) + c + 1)
                        z_chunk(1 - p, c)
                if before:
                    if not looped and g == 1:
                        pe.wait_ge(wo_split, 2)
                    if live:
                        pe.wait_ge(h_lo_ready, KC * g)
                    if live:
                        pe.wait_ge(y_ready, TILES * (g + 1))
                    if live:
                        out_tile(0)
                        out_tile(1)
                    else:
                        for lot in LAST_LOTS:
                            out_tiles_by_chunk(lot)
                    if not looped and g == GROUPS - 1:
                        out_tile(2)
                if live:
                    if not looped and g == 0:
                        pe.wait_ge(consts_ready, 4)
                    pe.wait_ge(attn_ready, 2 * (g + 1))
                    for t in range(TILES):
                        mm = nc.tensor.transpose(att_ps[:, t, :], attn[:, t, :], ident[:])
                    mm.then_inc(attnT_done, 1)
                if looped or 1 <= g < GROUPS:
                    if looped or g < GROUPS - 1:
                        out_tile(2)
                    out_tile(3)
                if live:
                    pe.wait_ge(attnT_ready, g + 1)
                    for c in range(KC):
                        if after:
                            pe.wait_ge(z_ready, KC * (g + 1) + c + 1)
                        for t in range(TILES):
                            o = slice(t * P, (t + 1) * P)
                            mm = nc.tensor.matmul(col_ps[c][:, o], y_sb[:, t, c * P:(c + 1) * P], attnT[:, o],
                                                  start=True, stop=True)
                        mm.then_inc(h_done, 1)
                if after:
                    for t in range(TILES):
                        if before:
                            pe.wait_ge(res_ready, TILES * (g - 1) + t + 1)
                        y_tile(1 - p, t)

            run_steps(pe, step)

            def typed_tile(g, q, n):
                pe.wait_ge(t_in, 32 * (n + 1))
                for c in range(KC):
                    for k in range(KC):
                        nc.tensor.matmul(col_ps[c][:, 0:P], m_sb[:, k, c * P:(c + 1) * P], t_xT[:, k, :],
                                         start=(k == 0), stop=(k == KC - 1))
                for k in range(KC):
                    nc.tensor.matmul(row_ps[:, 0, 0:HID], t_xT[:, k, :], gcn_sb[:, k, 0:HID],
                                     start=(k == 0), stop=(k == KC - 1))
                for k in range(KC):
                    mm = nc.tensor.matmul(row_ps[:, 1, 0:TYPES], t_xT[:, k, :], w1c2[:, k, :],
                                          start=(k == 0), stop=(k == KC - 1))
                mm.then_inc(t_front_done, 1)
                with pe.Fori(0, EDGE_TYPES) as e:
                    pe.wait_ge(t_vec, T_ALL * n + T_FRONT + T_TYPE * e + KC)
                    for k in range(KC):
                        mm = nc.tensor.matmul(att_ps[:, 0, :], t_zt[:, k, :], t_xT[:, k, :],
                                              start=(k == 0), stop=(k == KC - 1))
                    mm.then_inc(t_rel_done, 1)
                rest = T_ALL * n + T_FRONT + EDGE_TYPES * T_TYPE
                pe.wait_ge(t_vec, rest + 6)
                nc.tensor.transpose(att_ps[:, 1, :], attn[:, 0, :], ident[:]).then_inc(t_attnT_done, 1)
                pe.wait_ge(t_vec, rest + 7)
                for c in range(KC):
                    mm = nc.tensor.matmul(col_ps[c][:, 0:P], t_y[:, c * P:(c + 1) * P], t_attnT, start=True, stop=True)
                mm.then_inc(t_h_done, 1)
                pe.wait_ge(t_relu_done, KC * (n + 1))
                for k in range(KC):
                    mm = nc.tensor.matmul(row_ps[:, 0, 0:HID], t_h[:, k, :], wo_sb[:, k, :],
                                          start=(k == 0), stop=(k == KC - 1))
                mm.then_inc(t_out_done, 1)

            def typed_first():
                pe.wait_ge(t_m_ready, 1)

            typed_pass(pe, typed_tile, typed_first)


def kernel(**inputs):
    import numpy as np
    import concourse.bacc as bacc
    from concourse import mybir as mb
    from concourse.bass_utils import run_bass_kernel_spmd

    pre = "L0_gnn_"
    x = np.asarray(inputs["x"])
    adj = np.asarray(inputs["adj"])
    graphs, nodes, hid = x.shape
    kc, tiles = hid // 128, 4
    tok = tiles * 128
    groups = graphs * nodes // tok
    w1, w2 = np.asarray(inputs[pre + "W1_w"]), np.asarray(inputs[pre + "W2_w"])

    def rows(w):
        return w.reshape(-1, 128, w.shape[1]).transpose(1, 0, 2)

    def cols(b):
        return b.reshape(-1, 128).T

    laid = {
        "xT": x.reshape(groups, tok, kc, 128).transpose(0, 3, 2, 1),
        "xn": x.reshape(groups, tiles, 128, hid).transpose(0, 2, 1, 3),
        "adj": adj.reshape(groups, tiles, 128, nodes).transpose(0, 2, 1, 3),
        "w1T": rows(w1[:hid].T),
        "w2T": rows(w2[:hid].T),
        "dep": np.concatenate([w1[hid:], w2[hid:], np.asarray(inputs[pre + "dep_emb_table"]).T], axis=1),
        "gcn_w": rows(np.asarray(inputs[pre + "gcn_w"])),
        "wo_w": rows(np.asarray(inputs[pre + "Wo_w"])),
        "bias_cols": np.stack([cols(np.asarray(inputs[pre + b])) for b in ("W1_b", "W2_b", "gcn_b")], axis=1),
        "wo_b": np.asarray(inputs[pre + "Wo_b"]),
    }
    nc = bacc.Bacc("TRN2", target_bir_lowering=False, num_devices=1)
    arrays, args = {}, []
    for name, a in laid.items():
        a = np.ascontiguousarray(a)
        arrays[f"in_{name}_dram"] = a
        args.append(nc.dram_tensor(f"in_{name}_dram", a.shape, mb.dt.from_np(a.dtype), kind="ExternalInput").ap())
    args.append(nc.dram_tensor("out_0_dram", (groups, 128, tiles, hid), mb.dt.float32, kind="ExternalOutput").ap())
    adj_resnorm_kernel(nc, *args)
    r = run_bass_kernel_spmd(nc, [arrays], core_ids=[0])
    got = r.results[0]["out_0_dram"]
    return got.reshape(groups, 128, tiles, hid).transpose(0, 2, 1, 3).reshape(graphs, nodes, hid)
```
